# Optimizing a Trainium2 kernel written in Bass

```python
import numpy as np
import jax
import jax.numpy as jnp

def _softmax(x, axis=-1):
    return jax.nn.softmax(x, axis=axis)
def _gelu(x):
    return jax.nn.gelu(x, approximate=True)
def _silu(x):
    return jax.nn.silu(x)
def _sigmoid(x):
    return jax.nn.sigmoid(x)
def _layernorm(x, axis=-1, eps=1e-5):
    m = jnp.mean(x, axis=axis, keepdims=True)
    v = jnp.var(x, axis=axis, keepdims=True)
    return (x - m) / jnp.sqrt(v + eps)
def _scatter_add(tgt, idx, src, axis=0):
    return tgt.at[idx].add(src)
def _segment_sum(src, seg, n):
    return jax.ops.segment_sum(src, seg, n)

kernel_name = 'mk_conv_preact_d2_conv_nchw384_5fe62c'

def setup_inputs(seed: int = 0):
    np.random.seed(seed)
    _w = jnp.asarray
    def _rec_inputs():
        import jax
        import jax.numpy as jnp
        _gk = jax.random.key(seed)
        x = -0.0001836 + 1 * jax.random.normal(jax.random.fold_in(_gk, 1), (8, 384, 128, 128), jnp.float32)
        return x
    x = _rec_inputs()
    def _L0_conv_setup():
        import jax, jax.numpy as jnp
        import numpy as np
        from jax import lax
        C = 384
        key = jax.random.key(seed)
        k1, k2 = jax.random.split(key)
        x = jax.random.normal(k1, (16, C, 128, 128), dtype=jnp.float32)
        k = jax.random.normal(k2, (C, 1, 3, 3), dtype=jnp.float32)
        return {'x': x, 'k': k}
    _L0_conv_all = _L0_conv_setup()
    _L0_conv_in = {k: v for k, v in _L0_conv_all.items() if k in ('k', )}
    del _L0_conv_all

    def _L1_conv_setup():
        import jax, jax.numpy as jnp
        import numpy as np
        STRIDE = 1
        PAD = 3

        def _dwconv(x, w, stride, pad):
            C = x.shape[1]
            return jax.lax.conv_general_dilated(x, w, window_strides=(stride, stride), padding=[(pad, pad), (pad, pad)], dimension_numbers=('NCHW', 'OIHW', 'NCHW'), feature_group_count=C)
        key = jax.random.key(seed)
        k1, k2 = jax.random.split(key)
        x = jax.random.normal(k1, (16, 384, 64, 64), dtype=jnp.float32)
        k_sz = 7
        fan_out = 1 * k_sz * k_sz
        std = np.sqrt(2.0 / fan_out).astype(np.float32)
        weight = jax.random.normal(k2, (384, 1, k_sz, k_sz), dtype=jnp.float32) * std
        return {'x': x, 'weight': weight}
    _L1_conv_all = _L1_conv_setup()
    _L1_conv_in = {k: v for k, v in _L1_conv_all.items() if k in ('weight', )}
    del _L1_conv_all

    return {
        "x": x,
        "L0_conv_k": _L0_conv_in["k"],
        "L1_conv_weight": _L1_conv_in["weight"],
    }

def reference(x, L0_conv_k, L1_conv_weight):
    import jax
    import jax.numpy as jnp
    def _L0_conv_ref(x, k):
        import jax, jax.numpy as jnp
        import numpy as np
        from jax import lax
        C = 384
        return lax.conv_general_dilated(x, k, window_strides=(1, 1), padding=((1, 1), (1, 1)), rhs_dilation=(1, 1), dimension_numbers=('NCHW', 'OIHW', 'NCHW'), feature_group_count=C)

    def _L1_conv_ref(x, weight):
        import jax, jax.numpy as jnp
        import numpy as np
        STRIDE = 1
        PAD = 3

        def _dwconv(x, w, stride, pad):
            C = x.shape[1]
            return jax.lax.conv_general_dilated(x, w, window_strides=(stride, stride), padding=[(pad, pad), (pad, pad)], dimension_numbers=('NCHW', 'OIHW', 'NCHW'), feature_group_count=C)
        w_sym = (weight + jnp.rot90(weight, k=1, axes=(2, 3)) + jnp.rot90(weight, k=2, axes=(2, 3)) + jnp.rot90(weight, k=3, axes=(2, 3))) * 0.25
        return _dwconv(x, w_sym, STRIDE, PAD)

    def _gn(v, G=32, eps=1e-5):
        B_, C_, H_, W_ = v.shape
        g = v.reshape(B_, G, C_ // G, H_, W_)
        m = jnp.mean(g, axis=(2, 3, 4), keepdims=True)
        s = jnp.var(g, axis=(2, 3, 4), keepdims=True)
        return ((g - m) / jnp.sqrt(s + eps)).reshape(v.shape)

    def _ln_c(v, eps=1e-6):
        m = jnp.mean(v, axis=1, keepdims=True)
        s = jnp.var(v, axis=1, keepdims=True)
        return (v - m) / jnp.sqrt(s + eps)

    def _ln_t(v, eps=1e-5):
        m = jnp.mean(v, axis=-1, keepdims=True)
        s = jnp.var(v, axis=-1, keepdims=True)
        return (v - m) / jnp.sqrt(s + eps)

    def _to_tokens(v):
        B_, C_, H_, W_ = v.shape
        return v.reshape(B_, C_, H_ * W_).transpose(0, 2, 1)
    def _from_tokens(t, like):
        B_, C_, H_, W_ = like.shape
        return t.transpose(0, 2, 1).reshape(B_, C_, H_, W_)

    x = x + _L0_conv_ref(_gn(x), L0_conv_k)
    x = x + _L1_conv_ref(_gn(x), L1_conv_weight)
    return x


_drawn_inputs = setup_inputs


def setup_inputs(seed=0):
    import zlib

    import numpy as np

    out = dict(_drawn_inputs(seed))
    spreads = {}
    factors = {}
    for name, (base, spread) in spreads.items():
        noise = np.random.default_rng([zlib.crc32(name.encode()), seed]).standard_normal(out[name].shape)
        drawn = base * np.exp(spread * noise) if base else spread * noise
        out[name] = jnp.asarray(drawn.astype(out[name].dtype))
    for name, factor in factors.items():
        out[name] = (out[name] * factor).astype(out[name].dtype)
    return out
```

```python
from contextlib import ExitStack

import numpy as np

import concourse.bass as bass
from concourse import mybir

F32, F16, BF16 = mybir.dt.float32, mybir.dt.float16, mybir.dt.bfloat16
ALU = mybir.AluOpType
ACT = mybir.ActivationFunctionType
AXX = mybir.AxisListType.X

P = 128
W = 128
GC = 12
NI = 4
CC = 4
CPU_ = GC // CC
RING = 4
BODY = RING * CPU_

K1, K2 = 3, 7
P1 = W + 4
O1 = 2
P2 = W + 4
O2 = 4
L1 = NI * P1
L2 = NI * P2 + 4

BL = 32
NB = P // BL
WIN = 42
HALO = 5
EDGE = 36
ZS, WS = 64.0, 256.0
EPS = 1e-5

Q = 32
QW = Q + K1 - 1
V1P = Q + QW - 1
V1 = V1P * K1 * 2
B1 = P * K1 * 2
R1 = QW * K1 * 2
V2P = WIN + BL - 1
V2 = V2P * K2
B2 = BL * K2


def conv_program(nc, x, k1_in, k2_in, out):
    G = x.shape[1] // GC
    HALVES = x.shape[0] // NI
    UNITS = G * HALVES
    NCH = UNITS * CPU_
    GCH = HALVES * CPU_
    assert HALVES == 2 and NCH % BODY == 0 and NCH >= 3 * BODY

    v1_all = nc.dram_tensor("v1_all", (G, GC * V1), F16, kind="Internal").ap()
    v2_all = nc.dram_tensor("v2_all", (G, 2 * GC * V2), F16, kind="Internal").ap()
    v1_cur = nc.dram_tensor("v1_cur", (1, GC * V1), F16, kind="Internal").ap()
    v2_cur = nc.dram_tensor("v2_cur", (1, 2 * GC * V2), F16, kind="Internal").ap()
    rows1 = nc.dram_tensor("rows1", (GC, Q, R1), F16, kind="Internal").ap()
    rows2 = nc.dram_tensor("rows2", (2 * GC, WIN, B2), F16, kind="Internal").ap()

    with ExitStack() as ctx:
        def sb(name, shape, dt):
            return ctx.enter_context(nc.sbuf_tensor(name, shape, dt))

        def sem(name):
            return ctx.enter_context(nc.semaphore(name))

        X = sb("X", [P, RING, GC, NI, W], F32)
        H1 = sb("H1", [P, 2, 2, CC, L1], F16)
        H2 = sb("H2", [P, 2, 2, CC, L2], F16)
        BT = sb("BT", [P, 2, NB, CC, L2], F16)
        Z = sb("Z", [P, NI, CC * W], F32)
        DUMP = sb("DUMP", [P, 2, CC * W], BF16)
        BAND1 = sb("BAND1", [P, GC, B1], F16)
        BAND2 = sb("BAND2", [P, GC, B2], F16)
        BN = sb("BN", [P, CPU_, NI, 6], F32)
        MQ1 = sb("MQ1", [P, NI, 2], F32)
        SS = sb("SS", [P, CPU_, NI, 2], F32)
        ST = sb("ST", [P, 2, NI, 2], F32)
        TMP = sb("TMP", [P, 2, 6, NI], F32)
        RB = sb("RB", [P, 2, 2, 2, NI], F32)
        SC = sb("SC", [P, 2, G], F32)
        ONES1 = sb("ONES1", [P, P], F32)
        ONES2 = sb("ONES2", [P, P], F32)
        PS = ctx.enter_context(nc.psum_tensor("PS", [P, 8, 512], F32))
        PA, PB = PS[:, 0:4, :], PS[:, 4:8, :]
        PST = PS[:, 7, 0:2 * NI]

        wk = X[0:G, RING - 1, :, :, :].rearrange("g b c d -> g (b c d)")
        v1_sb = wk[:, 0:GC * V1 // 2].bitcast(F16)
        at = [GC * V1 // 2]

        def work(n):
            at[0] += n
            assert at[0] <= GC * NI * W
            return wk[:, at[0] - n:at[0]]

        NW1, NW2 = GC * K1 * K1, GC * K2 * K2
        w1_sb, w1_t = work(NW1), work(NW1)
        w2_sb, rot_a, rot_b = work(NW2), work(NW2), work(NW2)
        w2_sum = work(NW2)
        mx = work(2)
        inv = work(2)
        diag = work(2 * G)
        onesg = work(P)
        bt2 = BT[0:G, :, :, :, :].rearrange("g a b c d -> g (a b c d)")
        v2_sb = bt2[:, 0:2 * GC * V2]
        v2h_sb, v2l_sb = v2_sb[:, 0:GC * V2], v2_sb[:, GC * V2:2 * GC * V2]

        taps_loaded = sem("taps_loaded")
        zeroed = sem("zeroed")
        prep = sem("prep")
        scales_summed = sem("scales_summed")
        vectors_stored = sem("vectors_stored")
        blocks_zeroed = sem("blocks_zeroed")
        passed = sem("passed")
        x_loaded = [sem(f"x_loaded{r}") for r in range(RING)]
        stored = [sem(f"stored{r}") for r in range(RING)]
        gathered = [sem(f"gathered{q}") for q in range(2)]
        v1_ready, v2_ready = sem("v1_ready"), sem("v2_ready")
        rows1_cut, rows2_cut = sem("rows1_cut"), sem("rows2_cut")
        band1_loaded = [sem(f"band1_loaded{c}") for c in range(CPU_)]
        band2_loaded = [sem(f"band2_loaded{c}") for c in range(CPU_)]
        bn_done = sem("bn_done")
        mq_ready = sem("mq_ready")
        fin = [sem("fin1"), sem("fin2")]
        summed = [sem("summed1"), sem("summed2")]
        root = [sem("root1"), sem("root2")]
        normed = [sem("normed1"), sem("normed2")]
        hi_done = [sem("hi_done1"), sem("hi_done2")]
        lo_done = [sem("lo_done1"), sem("lo_done2")]
        conv1_done, conv2_done = sem("conv1_done"), sem("conv2_done")
        y_done = sem("y_done")
        squared = sem("squared")
        out_done = sem("out_done")

        PREP = 3 * (K2 + 1) + 2 * 3 + 4 + 2 * (K1 + K2) + 2
        FIN = 10

        def ring(n):
            return (n // CPU_) % RING

        def xs(n, img):
            c = n % CPU_
            return X[:, ring(n), c * CC:(c + 1) * CC, img, :]

        def flat32(tile):
            dims = " ".join("abcdef"[:len(tile.shape) - 1])
            return tile[:].rearrange(f"p {dims} -> p ({dims})").bitcast(F32)

        def part(H, n, which, img, off, pitch):
            return H[:, n % 2, which, :, off + img * pitch:off + img * pitch + W]

        def walk(eng, slot):
            for t in range(-5, BODY):
                slot(t, lambda n: n)
            with eng.Fori(1, NCH // BODY - 1) as i:
                for t in range(BODY):
                    slot(t + BODY, lambda n: n - BODY + i * BODY)
            for t in range(NCH - BODY, NCH + 6):
                slot(t, lambda n: n)

        def wait_apart(eng, semaphore, value):
            eng.wait_ge(semaphore, value)
            if not isinstance(value, int):
                eng.sem_inc(passed, 1)

        def real(n):
            return 0 <= n < NCH

        block = ctx.enter_context(nc.Block())

        @block.sync
        def _(sp):
            sp.dma_start(w1_sb, k1_in.rearrange("(g c) o i j -> g (c o i j)", c=GC)).then_inc(taps_loaded, 16)
            sp.dma_start(w2_sb, k2_in.rearrange("(g c) o i j -> g (c o i j)", c=GC)).then_inc(taps_loaded, 16)

            def cut_rows(rows, cur, length, pitch):
                chs, count, width = rows.shape
                return sp.dma_start(rows, bass.AP(cur.tensor, cur.offset + (count - 1) * pitch,
                                                  [[length, chs], [-pitch, count], [1, width]]))

            def slot(t, at):
                n = t + 5
                if real(n) and n % GCH == 0:
                    g = at(n) // GCH
                    if n == 0:
                        sp.wait_ge(vectors_stored, 32)
                    else:
                        wait_apart(sp, rows1_cut, g * 16)
                    sp.dma_start(v1_cur, v1_all[bass.ds(g, 1), :]).then_inc(v1_ready, 16)
                n = t + 3
                if real(n) and n % GCH == 0:
                    g = at(n) // GCH
                    wait_apart(sp, v1_ready, g * 16 + 16)
                    if n > 0:
                        for c in range(CPU_):
                            wait_apart(sp, band1_loaded[c], g * 64)
                    cut_rows(rows1, v1_cur, V1, 2 * K1).then_inc(rows1_cut, 16)
                n = t + 2
                if real(n) and n % GCH < CPU_:
                    c = n % CPU_
                    g = at(n - c) // GCH
                    wait_apart(sp, rows1_cut, g * 16 + 16)
                    if n >= GCH:
                        wait_apart(sp, conv1_done, at(n) - CPU_ + 1)
                    elif n == 0:
                        sp.wait_ge(zeroed, 9)
                    for q in range(P // Q):
                        m0, m1 = max(q * Q - 1, 0), min((q + 1) * Q + 1, P)
                        k0 = (m0 - (q * Q - 1)) * 2 * K1
                        sp.dma_start(BAND1[q * Q:(q + 1) * Q, c * CC:(c + 1) * CC, m0 * 2 * K1:m1 * 2 * K1],
                                     rows1[c * CC:(c + 1) * CC, :, k0:k0 + (m1 - m0) * 2 * K1]
                                     .rearrange("c r k -> r c k")).then_inc(band1_loaded[c], 16)
                n = t
                if real(n) and n % GCH == 0:
                    g = at(n) // GCH
                    if n > 0:
                        wait_apart(sp, rows2_cut, g * 16)
                    sp.dma_start(v2_cur, v2_all[bass.ds(g, 1), :]).then_inc(v2_ready, 16)
                n = t - 1
                if real(n) and n % GCH == 0:
                    g = at(n) // GCH
                    wait_apart(sp, v2_ready, g * 16 + 16)
                    if n > 0:
                        for c in range(CPU_):
                            wait_apart(sp, band2_loaded[c], g * 48)
                    cut_rows(rows2, v2_cur, V2, K2).then_inc(rows2_cut, 16)
                n = t - 2
                if real(n) and n % GCH < CPU_:
                    c = n % CPU_
                    g = at(n - c) // GCH
                    wait_apart(sp, rows2_cut, g * 16 + 16)
                    if n >= GCH:
                        wait_apart(sp, conv2_done, at(n) - CPU_ + 1)
                    for k, which in enumerate((0, 0, 1)):
                        r = which * GC + c * CC
                        sp.dma_start(BAND2[k * WIN:(k + 1) * WIN, c * CC:(c + 1) * CC, :],
                                     rows2[r:r + CC, :, :].rearrange("c r k -> r c k")
                                     ).then_inc(band2_loaded[c], 16)
                n = t - 5
                if real(n):
                    c, half = n % CPU_, (n // CPU_) % HALVES
                    ch0 = (at(n - n % GCH) // GCH) * GC + c * CC
                    wait_apart(sp, out_done, at(n) + 1)
                    for img in range(NI):
                        dst = out[half * NI + img, bass.ds(ch0, CC), :, :].rearrange("c h w -> h c w")
                        sp.dma_start(dst, xs(n, img)).then_inc(stored[ring(n)], 16)
                n = t - 3
                if real(n):
                    if n < 2:
                        sp.wait_ge(blocks_zeroed, 1)
                    else:
                        wait_apart(sp, conv2_done, at(n) - 1)
                    wait_apart(sp, lo_done[1], NI * at(n) + NI)
                    q = n % 2
                    for b in range(NB):
                        lo_row = b * BL - HALO
                        if b == 0:
                            lo_row, rows = 0, EDGE
                        elif b == NB - 1:
                            lo_row, rows = P - EDGE, EDGE
                        else:
                            rows = WIN
                        r0 = lo_row - (b * BL - HALO)
                        for k, which in enumerate((0, 1, 0)):
                            sp.dma_start(BT[k * WIN + r0:k * WIN + r0 + rows, q, b, :, :],
                                         H2[lo_row:lo_row + rows, q, which, :, :]).then_inc(gathered[q], 16)
                n = t + 5
                if real(n) and n % CPU_ == 0 and n > 0:
                    u = n // CPU_
                    half = u % HALVES
                    if u == RING - 1:
                        sp.wait_ge(vectors_stored, 32)
                        sp.wait_ge(scales_summed, 1)
                    if u >= RING:
                        wait_apart(sp, stored[ring(n)], (at(n) // BODY) * (16 * NI * CPU_))
                    ch0 = (at(n - n % GCH) // GCH) * GC
                    for img in range(NI):
                        src = x[half * NI + img, bass.ds(ch0, GC), :, :].rearrange("c h w -> h c w")
                        sp.dma_start(X[:, ring(n), :, img, :], src).then_inc(x_loaded[ring(n)], 16)

            for img in range(NI):
                sp.dma_start(X[:, 0, :, img, :], x[img, 0:GC, :, :].rearrange("c h w -> h c w")
                             ).then_inc(x_loaded[0], 16)
            sp.wait_ge(prep, PREP)
            sp.dma_start(v1_all, v1_sb).then_inc(vectors_stored, 16)
            sp.dma_start(v2_all, v2_sb).then_inc(vectors_stored, 16)
            walk(sp, slot)
            for r in range(RING):
                sp.wait_ge(stored[r], NCH // BODY * 16 * NI * CPU_)

        @block.vector
        def _(dve):
            v = nc.vector
            done = [0]

            def step(ins):
                done[0] += 1
                ins.then_inc(prep, 1)

            def settle():
                dve.wait_ge(prep, done[0])

            dve.wait_ge(taps_loaded, 32)
            sq = lambda a: a.rearrange("g (c i j) -> g c i j", c=GC, i=K2)
            prev = w2_sb
            for turn in range(3):
                rot = (rot_a, rot_b, rot_a)[turn]
                for i in range(K2):
                    step(v.tensor_copy(sq(rot)[:, :, i, :], sq(prev)[:, :, :, K2 - 1 - i]))
                settle()
                step(v.tensor_tensor(w2_sum, w2_sb if turn == 0 else w2_sum, rot, ALU.add))
                settle()
                prev = rot
            for k, (w, t) in enumerate(((w1_sb, w1_t), (w2_sum, rot_b))):
                step(v.tensor_scalar(t, w, -1.0, None, ALU.mult))
                settle()
                step(v.tensor_tensor(t, t, w, ALU.max))
                settle()
                step(v.reduce_max(mx[:, k:k + 1], t, AXX))
            settle()
            step(v.tensor_scalar(mx, mx, 1e-30, None, ALU.max))
            settle()
            step(v.reciprocal(inv, mx))
            settle()
            step(v.tensor_scalar(w1_t, w1_sb, inv[:, 0:1], WS, ALU.mult, ALU.mult))
            step(v.tensor_scalar(rot_b, w2_sum, inv[:, 1:2], WS, ALU.mult, ALU.mult))
            settle()
            dve.wait_ge(zeroed, 2)
            w1v = w1_t.rearrange("g (c i j) -> g c i j", c=GC, i=K1)
            w2v = sq(rot_b)
            v1v = v1_sb.rearrange("g (c p j s) -> g c p j s", c=GC, p=V1P, j=K1)
            v2hv = v2h_sb.rearrange("g (c p j) -> g c p j", c=GC, p=V2P)
            v2lv = v2l_sb.rearrange("g (c p j) -> g c p j", c=GC, p=V2P)
            for dy in range(K1):
                step(v.tensor_copy(v1v[:, :, Q + 1 - dy, :, 0], w1v[:, :, dy, :]))
            for dy in range(K2):
                step(v.tensor_copy(v2hv[:, :, WIN - K1 - dy, :], w2v[:, :, dy, :]))
            settle()
            for dy in range(K1):
                step(v.tensor_tensor(v1v[:, :, Q + 1 - dy, :, 1], w1v[:, :, dy, :], v1v[:, :, Q + 1 - dy, :, 0],
                                     ALU.subtract))
            for dy in range(K2):
                step(v.tensor_tensor(v2lv[:, :, WIN - K1 - dy, :], w2v[:, :, dy, :],
                                     v2hv[:, :, WIN - K1 - dy, :], ALU.subtract))
            dve.wait_ge(zeroed, 5)
            for k in range(2):
                step(v.tensor_scalar(diag[:, k * G:(k + 1) * G], diag[:, k * G:(k + 1) * G], mx[:, k:k + 1],
                                     None, ALU.mult))
            assert done[0] == PREP
            dve.wait_ge(scales_summed, 1)
            step(v.tensor_scalar(SC[:, 0, :], PS[:, 7, 0:G], 1.0 / (ZS * WS), None, ALU.mult))
            step(v.tensor_scalar(SC[:, 1, :], PS[:, 7, G:2 * G], 0.25 / (ZS * WS), None, ALU.mult))
            settle()

            def finish(layer, u0, u):
                f, tmp, rb = fin[layer], TMP[:, layer], RB[:, layer, u0 % 2]
                mean, msq = ST[:, layer, :, 0], ST[:, layer, :, 1]
                steps = [0]

                def nxt(ins, wait=True):
                    steps[0] += 1
                    ins.then_inc(f, 1)
                    if wait:
                        dve.wait_ge(f, u * FIN + steps[0])

                dve.wait_ge(summed[layer], u + 1)
                nxt(v.tensor_copy(ST[:, layer, :, :], PST.rearrange("p (i s) -> p i s", s=2)))
                nxt(v.tensor_tensor(tmp[:, 0], mean, mean, ALU.mult))
                nxt(v.tensor_tensor(tmp[:, 1], msq, tmp[:, 0], ALU.subtract))
                nxt(v.tensor_scalar(tmp[:, 2], tmp[:, 1], 0.0, EPS, ALU.max, ALU.add))
                dve.wait_ge(root[layer], u + 1)
                nxt(v.reciprocal(tmp[:, 4], tmp[:, 3]))
                nxt(v.tensor_tensor(tmp[:, 0], tmp[:, 2], tmp[:, 4], ALU.mult))
                nxt(v.tensor_tensor(tmp[:, 1], tmp[:, 0], tmp[:, 4], ALU.mult))
                nxt(v.tensor_scalar(tmp[:, 5], tmp[:, 1], -0.5, 1.5, ALU.mult, ALU.add))
                nxt(v.scalar_tensor_tensor(rb[:, 0], tmp[:, 4], ZS, tmp[:, 5], ALU.mult, ALU.mult))
                nxt(v.scalar_tensor_tensor(rb[:, 1], mean, -1.0, rb[:, 0], ALU.mult, ALU.mult))
                assert steps[0] == FIN

            def slot(t, at):
                n = t - 5
                if real(n):
                    c = n % CPU_
                    y = X[:, ring(n), c * CC:(c + 1) * CC, :, :].rearrange("p c i w -> p (c i w)")
                    g = at(n - n % GCH) // GCH
                    dve.wait_ge(conv2_done, at(n) + 1)
                    v.scalar_tensor_tensor(y, PB.rearrange("p b w -> p (b w)"), SC[:, 1, bass.ds(g, 1)], y,
                                           ALU.mult, ALU.add).then_inc(out_done, 1)
                n = t - 3
                if real(n) and n % CPU_ == 0:
                    finish(1, n // CPU_, at(n) // CPU_)
                if real(n):
                    for img in range(NI):
                        m = NI * at(n) + img
                        dve.wait_ge(normed[1], m + 1)
                        dve.wait_ge(hi_done[1], m + 1)
                        v.tensor_tensor(part(H2, n, 1, img, O2, P2),
                                        Z[:, img, :].rearrange("p (c w) -> p c w", c=CC),
                                        part(H2, n, 0, img, O2, P2), ALU.subtract).then_inc(lo_done[1], 1)
                n = t + 1
                if real(n) and n % CPU_ == 0:
                    finish(0, n // CPU_, at(n) // CPU_)
                if real(n):
                    for img in range(NI):
                        m = NI * at(n) + img
                        dve.wait_ge(normed[0], m + 1)
                        dve.wait_ge(hi_done[0], m + 1)
                        v.tensor_tensor(part(H1, n, 1, img, O1, P1),
                                        Z[:, img, :].rearrange("p (c w) -> p c w", c=CC),
                                        part(H1, n, 0, img, O1, P1), ALU.subtract).then_inc(lo_done[0], 1)
                n = t
                if real(n):
                    c = n % CPU_
                    g = at(n - n % GCH) // GCH
                    dve.wait_ge(conv1_done, at(n) + 1)
                    for img in range(NI):
                        v.scalar_tensor_tensor(xs(n, img), PA[:, :, img * W:(img + 1) * W],
                                               SC[:, 0, bass.ds(g, 1)], xs(n, img), ALU.mult, ALU.add,
                                               accum_out=SS[:, c, img, 0:1]).then_inc(y_done, 1)
                n = t + 4
                if real(n):
                    c = n % CPU_
                    if c == 0:
                        dve.wait_ge(x_loaded[ring(n)], (at(n - n % BODY) // BODY + 1) * (16 * NI))
                    for img in range(NI):
                        v.bn_stats(BN[:, c, img, :], xs(n, img)).then_inc(bn_done, 1)
                    if c == CPU_ - 1:
                        wait_apart(dve, bn_done, NI * at(n) + NI)
                        u = at(n - c) // CPU_
                        for img in range(NI):
                            v.bn_aggr(MQ1[:, img, :], BN[:, :, img, :]).then_inc(mq_ready, 1)
                        dve.wait_ge(mq_ready, u * (NI + 2) + NI)
                        v.tensor_tensor(TMP[:, 0, 0], MQ1[:, :, 0], MQ1[:, :, 0], ALU.mult).then_inc(mq_ready, 1)
                        dve.wait_ge(mq_ready, u * (NI + 2) + NI + 1)
                        v.tensor_tensor(MQ1[:, :, 1], MQ1[:, :, 1], TMP[:, 0, 0], ALU.add).then_inc(mq_ready, 1)

            walk(dve, slot)

        @block.scalar
        def _(act):
            def normalise(layer, n, at):
                m = NI * at(n)
                for img in range(NI):
                    if layer == 1 and real(n + 3):
                        act.wait_ge(lo_done[0], m + 3 * NI + img + 1)
                    elif layer == 1:
                        act.wait_ge(lo_done[1], m - NI + img + 1)
                    elif real(n - 4):
                        act.wait_ge(lo_done[1], m - 4 * NI + img + 1)
                    elif n > 0:
                        act.wait_ge(lo_done[0], m - NI + img + 1)
                    rb = RB[:, layer, (n // CPU_) % 2]
                    nc.scalar.activation(Z[:, img, :].rearrange("p (c w) -> p c w", c=CC), xs(n, img),
                                         ACT.Identity, bias=rb[:, 1, img:img + 1],
                                         scale=rb[:, 0, img:img + 1]).then_inc(normed[layer], 1)

            def take_root(layer, u):
                act.wait_ge(fin[layer], u * FIN + 4)
                nc.scalar.activation(TMP[:, layer, 3], TMP[:, layer, 2], ACT.Sqrt).then_inc(root[layer], 1)

            def slot(t, at):
                n = t - 1
                if real(n):
                    for img in range(NI):
                        act.wait_ge(y_done, NI * at(n) + img + 1)
                        if n > 0 or img >= 2:
                            act.wait_ge(squared, NI * at(n) + img - 1)
                        nc.scalar.activation(DUMP[:, img % 2].rearrange("p (c w) -> p c w", c=CC), xs(n, img), ACT.Square,
                                             accum_out=SS[:, n % CPU_, img, 1:2]).then_inc(squared, 1)
                n = t - 3
                if real(n):
                    if n % CPU_ == 0:
                        take_root(1, at(n) // CPU_)
                        act.wait_ge(fin[1], (at(n) // CPU_) * FIN + FIN)
                    normalise(1, n, at)
                n = t + 1
                if real(n):
                    if n % CPU_ == 0:
                        take_root(0, at(n) // CPU_)
                        act.wait_ge(fin[0], (at(n) // CPU_) * FIN + FIN)
                    normalise(0, n, at)

            walk(act, slot)

        @block.gpsimd
        def _(pool):
            g = nc.gpsimd
            g.memset(v1_sb.bitcast(F32), 0.0).then_inc(zeroed, 1)
            g.memset(v2_sb.bitcast(F32), 0.0).then_inc(zeroed, 1)
            g.memset(diag, 0.0).then_inc(zeroed, 1)
            pool.wait_ge(zeroed, 3)
            for k in range(2):
                d = diag[:, k * G:(k + 1) * G]
                g.affine_select(out=d, in_=d, compare_op=ALU.not_equal, fill=1.0, base=0, pattern=[[-1, G]],
                                channel_multiplier=1).then_inc(zeroed, 1)
            g.memset(onesg, 1.0).then_inc(zeroed, 1)
            g.memset(ONES1[:], 1.0 / P).then_inc(zeroed, 1)
            g.memset(ONES2[:], 1.0 / (GC * P * W)).then_inc(zeroed, 1)
            for whole in (BAND1, H1, H2):
                g.memset(flat32(whole), 0.0).then_inc(zeroed, 1)
            pool.wait_ge(vectors_stored, 32)
            g.memset(flat32(BT), 0.0).then_inc(blocks_zeroed, 1)

            def high_parts(layer, n, at):
                H, off, pitch = ((H1, O1, P1), (H2, O2, P2))[layer]
                u = at(n - n % CPU_) // CPU_
                wait_apart(pool, fin[layer], u * FIN + FIN)
                if n >= 2:
                    if layer == 0:
                        wait_apart(pool, conv1_done, at(n) - 1)
                    else:
                        wait_apart(pool, gathered[n % 2], ((at(n) - n % 2) // 2) * (16 * 3 * NB))
                rb = RB[:, layer, (n // CPU_) % 2]
                for img in range(NI):
                    g.tensor_scalar(part(H, n, 0, img, off, pitch), xs(n, img), rb[:, 0, img:img + 1],
                                    rb[:, 1, img:img + 1], ALU.mult, ALU.add).then_inc(hi_done[layer], 1)

            def slot(t, at):
                if real(t - 3):
                    high_parts(1, t - 3, at)
                if real(t + 1):
                    high_parts(0, t + 1, at)

            walk(pool, slot)

        @block.tensor
        def _(pe):
            mm = nc.tensor.matmul
            pe.wait_ge(zeroed, 11)
            pe.wait_ge(prep, PREP)
            mm(PS[:, 7, 0:2 * G], onesg, diag, start=True, stop=True).then_inc(scales_summed, 1)
            pe.wait_ge(prep, PREP + 2)

            def slot(t, at):
                n = t
                for ch in range(CC):
                    if ch == 2:
                        u = t - 3
                        if real(u) and u % CPU_ == 0:
                            pe.wait_ge(squared, NI * at(u) + NI * CPU_)
                            if real(t - 5):
                                pe.wait_ge(out_done, at(t - 5) + 1)
                            for c in range(CPU_):
                                last = mm(PST, ONES2[:], SS[:, c].rearrange("p i s -> p (i s)"), start=c == 0,
                                          stop=c == CPU_ - 1)
                            last.then_inc(summed[1], 1)
                        u = t + 1
                        if real(u) and u % CPU_ == 0:
                            pe.wait_ge(mq_ready, (at(u) // CPU_ + 1) * (NI + 2))
                            if real(t - 5):
                                pe.wait_ge(out_done, at(t - 5) + 1)
                            mm(PST, ONES1[:], MQ1[:].rearrange("p i s -> p (i s)"), start=True,
                               stop=True).then_inc(summed[0], 1)
                    if not real(n):
                        continue
                    c = n % CPU_
                    if ch == 0:
                        pe.wait_ge(band1_loaded[c], (at(n - n % GCH) // GCH) * 64 + 64)
                        pe.wait_ge(lo_done[0], NI * at(n) + NI)
                        if n >= 1:
                            pe.wait_ge(y_done, NI * at(n))
                    band = BAND1[:, c * CC + ch, :].rearrange("p (m j s) -> p j s m", m=P, j=K1)
                    k = 0
                    for j in range(K1):
                        for which, ws in ((0, 0), (1, 0), (0, 1)):
                            data = H1[:, n % 2, which, ch, :].rearrange("p (i q) -> p i q", i=NI)
                            last = mm(PA[:, ch, :], band[:, j, ws, :], data[:, :, O1 - 1 + j:O1 - 1 + j + W],
                                      start=k == 0, stop=k == 3 * K1 - 1)
                            k += 1
                    if ch == CC - 1:
                        last.then_inc(conv1_done, 1)
                n = t - 4
                if real(n):
                    c = n % CPU_
                    pe.wait_ge(band2_loaded[c], (at(n - n % GCH) // GCH) * 48 + 48)
                    pe.wait_ge(gathered[n % 2], ((at(n) - n % 2) // 2 + 1) * (16 * 3 * NB))
                    if n >= 1:
                        pe.wait_ge(out_done, at(n))
                    for ch in range(CC):
                        if ch == CC - 1:
                            if real(t - 3) and (t - 3) % CPU_ == 0:
                                pe.wait_ge(fin[1], (at(t - 3) // CPU_) * FIN + 1)
                            if real(t + 1) and (t + 1) % CPU_ == 0:
                                pe.wait_ge(fin[0], (at(t + 1) // CPU_) * FIN + 1)
                        band = BAND2[0:3 * WIN, c * CC + ch, :].rearrange("p (m j) -> p j m", m=BL)
                        for j in range(K2):
                            for b in range(NB):
                                rows = BT[0:3 * WIN, n % 2, b, ch, O2 - K2 // 2 + j:]
                                rows = bass.AP(rows.tensor, rows.offset, [rows.ap[0], [P2, NI], [1, W]])
                                last = mm(PB[b * BL:(b + 1) * BL, ch, :], band[:, j, :],
                                          rows, start=j == 0, stop=j == K2 - 1, tile_position=(0, b * BL))
                    last.then_inc(conv2_done, 1)

            walk(pe, slot)


def kernel(**inputs):
    import numpy as _np
    import concourse.bacc as _bacc
    from concourse import mybir as _mybir
    from concourse.bass_utils import run_bass_kernel_spmd as _run

    nc = _bacc.Bacc("TRN2", target_bir_lowering=False, num_devices=1)
    arrays, args = {}, []
    for name in ("x", "L0_conv_k", "L1_conv_weight"):
        a = _np.ascontiguousarray(inputs[name])
        arrays[f"in_{name}"] = a
        args.append(nc.dram_tensor(f"in_{name}", a.shape, _mybir.dt.from_np(a.dtype), kind="ExternalInput").ap())
    shape = tuple(inputs["x"].shape)
    args.append(nc.dram_tensor("out_y", shape, _mybir.dt.float32, kind="ExternalOutput").ap())
    conv_program(nc, *args)
    r = _run(nc, [arrays], core_ids=[0])
    return r.results[0]["out_y"]
```

```python
from contextlib import ExitStack

import concourse.bass as bass
from concourse import mybir

F32, F16, BF16 = mybir.dt.float32, mybir.dt.float16, mybir.dt.bfloat16
ALU = mybir.AluOpType
ACT = mybir.ActivationFunctionType
AXX = mybir.AxisListType.X

P = 128
W = 128
GC = 12
NI = 4
CC = 4
CPU_ = GC // CC
RING = 4
BODY = RING * CPU_
AHEAD = 6
CONV2 = 4

K1, K2 = 3, 7
P1 = W + 4
O1 = 2
P2 = W + 4
O2 = 4
L1 = NI * P1
L2 = NI * P2 + 4

BL = 32
NB = P // BL
WIN = 42
HALO = 5
EDGE = 36
ZS, WS = 64.0, 256.0
EPS = 1e-5

Q = 32
QW = Q + K1 - 1
V1P = Q + QW - 1
V1 = V1P * K1 * 2
B1 = P * K1 * 2
R1 = QW * K1 * 2
V2P = WIN + BL - 1
V2 = V2P * K2
B2 = BL * K2


def conv_program(nc, x, k1_in, k2_in, out):
    G = x.shape[1] // GC
    HALVES = x.shape[0] // NI
    UNITS = G * HALVES
    NCH = UNITS * CPU_
    GCH = HALVES * CPU_
    assert HALVES == 2 and NCH % BODY == 0 and NCH >= 3 * BODY

    v1_all = nc.dram_tensor("v1_all", (G, GC * V1), F16, kind="Internal").ap()
    v2_all = nc.dram_tensor("v2_all", (G, 2 * GC * V2), F16, kind="Internal").ap()
    v1_cur = nc.dram_tensor("v1_cur", (1, GC * V1), F16, kind="Internal").ap()
    v2_cur = nc.dram_tensor("v2_cur", (1, 2 * GC * V2), F16, kind="Internal").ap()
    rows1 = nc.dram_tensor("rows1", (GC, Q, R1), F16, kind="Internal").ap()
    rows2 = nc.dram_tensor("rows2", (3 * WIN, GC, B2), F16, kind="Internal").ap()

    with ExitStack() as ctx:
        def sb(name, shape, dt):
            return ctx.enter_context(nc.sbuf_tensor(name, shape, dt))

        def sem(name):
            return ctx.enter_context(nc.semaphore(name))

        X = sb("X", [P, RING, GC, NI, W], F32)
        H1 = sb("H1", [P, 2, 2, CC, L1], F16)
        H2 = sb("H2", [P, 2, 2, CC, L2], F16)
        BT = sb("BT", [P, 2, NB, CC, L2], F16)
        Z = sb("Z", [P, NI, CC * W], F32)
        DUMP = sb("DUMP", [P, 2, CC * W], BF16)
        BAND1 = sb("BAND1", [P, GC, B1], F16)
        BAND2 = sb("BAND2", [P, GC, B2], F16)
        BN = sb("BN", [P, CPU_, NI, 6], F32)
        MQ1 = sb("MQ1", [P, NI, 2], F32)
        SS = sb("SS", [P, CPU_, NI, 2], F32)
        ST = sb("ST", [P, 2, NI, 2], F32)
        TMP = sb("TMP", [P, 2, 6, NI], F32)
        RB = sb("RB", [P, 2, 2, 2, NI], F32)
        SC = sb("SC", [P, 2, G], F32)
        ONES1 = sb("ONES1", [P, P], F32)
        ONES2 = sb("ONES2", [P, P], F32)
        PS = ctx.enter_context(nc.psum_tensor("PS", [P, 8, 512], F32))
        PA, PB = PS[:, 0:4, :], PS[:, 4:8, :]
        PST = PS[:, 7, 0:CPU_ * 2 * NI]

        wk = X[0:G, RING - 1, :, :, :].rearrange("g b c d -> g (b c d)")
        v1_sb = wk[:, 0:GC * V1 // 2].bitcast(F16)
        at = [GC * V1 // 2]

        def work(n):
            at[0] += n
            assert at[0] <= GC * NI * W
            return wk[:, at[0] - n:at[0]]

        NW1, NW2 = GC * K1 * K1, GC * K2 * K2
        w1_sb, w1_t = work(NW1), work(NW1)
        w2_sb, rot_a, rot_b = work(NW2), work(NW2), work(NW2)
        w2_sum = work(NW2)
        mx = work(2)
        inv = work(2)
        diag = work(2 * G)
        onesg = work(P)
        bt2 = BT[0:G, :, :, :, :].rearrange("g a b c d -> g (a b c d)")
        v2_sb = bt2[:, 0:2 * GC * V2]

        taps_loaded = [sem("taps_loaded1"), sem("taps_loaded2")]
        zeroed = sem("zeroed")
        prep = [sem("prep1"), sem("prep2")]
        scales_summed = sem("scales_summed")
        vectors_stored = [sem("vectors_stored1"), sem("vectors_stored2")]
        blocks_zeroed = sem("blocks_zeroed")
        passed = sem("passed")
        x_loaded = [sem(f"x_loaded{r}") for r in range(BODY)]
        stored = [sem(f"stored{r}") for r in range(BODY)]
        gathered = [sem(f"gathered{q}") for q in range(2)]
        v1_ready, v2_ready = sem("v1_ready"), sem("v2_ready")
        rows1_cut, rows2_cut = sem("rows1_cut"), sem("rows2_cut")
        band1_loaded = [sem(f"band1_loaded{c}") for c in range(CPU_)]
        band2_loaded = [sem(f"band2_loaded{c}") for c in range(CPU_)]
        bn_done = sem("bn_done")
        mq_ready = sem("mq_ready")
        fin = [sem("fin1"), sem("fin2")]
        summed = [sem("summed1"), sem("summed2")]
        root = [sem("root1"), sem("root2")]
        normed = [sem("normed1"), sem("normed2")]
        hi_done = [sem("hi_done1"), sem("hi_done2")]
        lo_done = [sem("lo_done1"), sem("lo_done2")]
        conv1_done, conv2_done = sem("conv1_done"), sem("conv2_done")
        y_done = sem("y_done")
        squared = sem("squared")
        out_done = sem("out_done")
        bank_free = sem("bank_free")

        PREP = (3 + 3 + 2 * K1 + 1, 3 * (K2 + 1) + 3 + 3 + 2 * K2 + 1)
        FIN = 10

        def ring(n):
            return (n // CPU_) % RING

        def xs(n, img):
            c = n % CPU_
            return X[:, ring(n), c * CC:(c + 1) * CC, img, :]

        def flat32(tile):
            dims = " ".join("abcdef"[:len(tile.shape) - 1])
            return tile.rearrange(f"p {dims} -> p ({dims})").bitcast(F32)

        def part(H, n, which, img, off, pitch):
            return H[:, n % 2, which, :, off + img * pitch:off + img * pitch + W]

        def banks2(n):
            return PA if n in (NCH - CONV2, NCH - CONV2 + 2) else PB

        def walk(eng, slot):
            for t in range(-5, BODY):
                slot(t, lambda n: n)
            with eng.Fori(1, NCH // BODY - 1) as i:
                for t in range(BODY):
                    slot(t + BODY, lambda n: n - BODY + i * BODY)
            for t in range(NCH - BODY, NCH + 6):
                slot(t, lambda n: n)

        def wait_apart(eng, semaphore, value):
            eng.wait_ge(semaphore, value)
            if not isinstance(value, int):
                eng.sem_inc(passed, 1)

        def real(n):
            return 0 <= n < NCH

        block = ctx.enter_context(nc.Block())

        @block.sync
        def _(sp):
            sp.dma_start(w1_sb, k1_in.rearrange("(g c) o i j -> g (c o i j)", c=GC)).then_inc(taps_loaded[0], 16)
            sp.dma_start(w2_sb, k2_in.rearrange("(g c) o i j -> g (c o i j)", c=GC)).then_inc(taps_loaded[1], 16)

            def cut_rows(rows, cur, length, pitch):
                chs, count, width = rows.shape
                return sp.dma_start(rows, bass.AP(cur.tensor, cur.offset + (count - 1) * pitch,
                                                  [[length, chs], [-pitch, count], [1, width]]))

            def load(n, at):
                c, half = n % CPU_, (n // CPU_) % HALVES
                ch0 = (at(n - n % GCH) // GCH) * GC + c * CC
                for img in range(NI):
                    src = x[half * NI + img, bass.ds(ch0, CC), :, :].rearrange("c h w -> h c w")
                    sp.dma_start(xs(n, img), src).then_inc(x_loaded[n % BODY], 16)

            def store(n, at):
                if real(n):
                    c, half = n % CPU_, (n // CPU_) % HALVES
                    ch0 = (at(n - n % GCH) // GCH) * GC + c * CC
                    wait_apart(sp, bank_free, at(n) + 1)
                    wait_apart(sp, out_done, at(n) + 1)
                    for img in range(NI):
                        dst = out[half * NI + img, bass.ds(ch0, CC), :, :].rearrange("c h w -> h c w")
                        sp.dma_start(dst, xs(n, img)).then_inc(stored[n % BODY], 16)

            def slot(t, at):
                n = t + 5
                if real(n) and n % GCH == 0:
                    g = at(n) // GCH
                    if n == 0:
                        sp.wait_ge(vectors_stored[0], 16)
                    else:
                        wait_apart(sp, rows1_cut, g * 16)
                    sp.dma_start(v1_cur, v1_all[bass.ds(g, 1), :]).then_inc(v1_ready, 16)
                n = t + 3
                if real(n) and n % GCH == 0:
                    g = at(n) // GCH
                    wait_apart(sp, v1_ready, g * 16 + 16)
                    if n > 0:
                        for c in range(CPU_):
                            wait_apart(sp, band1_loaded[c], g * 64)
                    cut_rows(rows1, v1_cur, V1, 2 * K1).then_inc(rows1_cut, 16)
                n = t + 2
                if real(n) and n % GCH < CPU_:
                    c = n % CPU_
                    g = at(n - c) // GCH
                    wait_apart(sp, rows1_cut, g * 16 + 16)
                    if n >= GCH:
                        wait_apart(sp, conv1_done, at(n) - CPU_ + 1)
                    elif n == 0:
                        sp.wait_ge(zeroed, 8)
                    for q in range(P // Q):
                        m0, m1 = max(q * Q - 1, 0), min((q + 1) * Q + 1, P)
                        k0 = (m0 - (q * Q - 1)) * 2 * K1
                        sp.dma_start(BAND1[q * Q:(q + 1) * Q, c * CC:(c + 1) * CC, m0 * 2 * K1:m1 * 2 * K1],
                                     rows1[c * CC:(c + 1) * CC, :, k0:k0 + (m1 - m0) * 2 * K1]
                                     .rearrange("c r k -> r c k")).then_inc(band1_loaded[c], 16)
                n = t
                if real(n) and n % GCH == 0:
                    g = at(n) // GCH
                    if n == 0:
                        sp.wait_ge(prep[1], PREP[1])
                        sp.dma_start(v2_all, v2_sb).then_inc(vectors_stored[1], 16)
                        sp.wait_ge(vectors_stored[1], 16)
                    else:
                        wait_apart(sp, rows2_cut, g * 48)
                    sp.dma_start(v2_cur, v2_all[bass.ds(g, 1), :]).then_inc(v2_ready, 16)
                n = t - 1
                if real(n) and n % GCH == 0:
                    g = at(n) // GCH
                    wait_apart(sp, v2_ready, g * 16 + 16)
                    if n > 0:
                        for c in range(CPU_):
                            wait_apart(sp, band2_loaded[c], g * 16)
                    for k, which in enumerate((0, 0, 1)):
                        cut_rows(rows2[k * WIN:(k + 1) * WIN].rearrange("r c k -> c r k"),
                                 v2_cur[:, which * GC * V2:(which + 1) * GC * V2], V2, K2).then_inc(rows2_cut, 16)
                n = t - 2
                if real(n) and n % GCH < CPU_:
                    c = n % CPU_
                    g = at(n - c) // GCH
                    wait_apart(sp, rows2_cut, g * 48 + 48)
                    if n >= GCH:
                        wait_apart(sp, conv2_done, at(n) - CPU_ + 1)
                    sp.dma_start(BAND2[0:3 * WIN, c * CC:(c + 1) * CC, :], rows2[:, c * CC:(c + 1) * CC, :]
                                 ).then_inc(band2_loaded[c], 16)
                if t <= NCH:
                    store(t - 5, at)
                n = t - 3
                if real(n):
                    if n < 2:
                        sp.wait_ge(blocks_zeroed, 1)
                    else:
                        wait_apart(sp, conv2_done, at(n) - 1)
                    wait_apart(sp, lo_done[1], NI * at(n) + NI)
                    q = n % 2
                    for b in range(NB):
                        lo_row = b * BL - HALO
                        if b == 0:
                            lo_row, rows = 0, EDGE
                        elif b == NB - 1:
                            lo_row, rows = P - EDGE, EDGE
                        else:
                            rows = WIN
                        r0 = lo_row - (b * BL - HALO)
                        for k, which in enumerate((0, 1, 0)):
                            sp.dma_start(BT[k * WIN + r0:k * WIN + r0 + rows, q, b, :, :],
                                         H2[lo_row:lo_row + rows, q, which, :, :]).then_inc(gathered[q], 16)
                if t > NCH:
                    store(t - 5, at)
                n = t + AHEAD
                if real(n) and n >= CPU_:
                    if n // CPU_ == RING - 1:
                        sp.wait_ge(vectors_stored[0], 16)
                        sp.wait_ge(vectors_stored[1], 16)
                        sp.wait_ge(scales_summed, 2)
                    if n >= BODY:
                        wait_apart(sp, stored[n % BODY], (at(n - n % BODY) // BODY) * (16 * NI))
                    load(n, at)

            for n in range(CPU_):
                load(n, lambda m: m)
            sp.wait_ge(prep[0], PREP[0])
            sp.dma_start(v1_all, v1_sb).then_inc(vectors_stored[0], 16)
            walk(sp, slot)
            for place in range(BODY):
                sp.wait_ge(stored[place], NCH // BODY * 16 * NI)

        @block.vector
        def _(dve):
            v = nc.vector
            done = [0, 0]
            w1v = w1_t.rearrange("g (c i j) -> g c i j", c=GC, i=K1)
            sq = lambda a: a.rearrange("g (c i j) -> g c i j", c=GC, i=K2)
            v1v = v1_sb.rearrange("g (c p j s) -> g c p j s", c=GC, p=V1P, j=K1)
            v2v = v2_sb.rearrange("g (s c p j) -> g s c p j", s=2, c=GC, p=V2P)

            def step(layer, ins):
                done[layer] += 1
                ins.then_inc(prep[layer], 1)

            def settle(layer):
                dve.wait_ge(prep[layer], done[layer])

            def add_rotations():
                prev = w2_sb
                for turn in range(3):
                    rot = (rot_a, rot_b, rot_a)[turn]
                    for i in range(K2):
                        step(1, v.tensor_copy(sq(rot)[:, :, i, :], sq(prev)[:, :, :, K2 - 1 - i]))
                    settle(1)
                    step(1, v.tensor_tensor(w2_sum, w2_sb if turn == 0 else w2_sum, rot, ALU.add))
                    settle(1)
                    prev = rot

            def prepare(layer):
                w, t, wt = ((w1_sb, w1_t, w1_t), (w2_sum, rot_b, rot_b))[layer]
                m, r = mx[:, layer:layer + 1], inv[:, layer:layer + 1]
                step(layer, v.tensor_scalar(t, w, -1.0, None, ALU.mult))
                settle(layer)
                step(layer, v.tensor_tensor(t, t, w, ALU.max))
                settle(layer)
                step(layer, v.reduce_max(m, t, AXX))
                settle(layer)
                step(layer, v.tensor_scalar(m, m, 1e-30, None, ALU.max))
                settle(layer)
                step(layer, v.reciprocal(r, m))
                settle(layer)
                step(layer, v.tensor_scalar(wt, w, r, WS, ALU.mult, ALU.mult))
                d = diag[:, layer * G:(layer + 1) * G]
                dve.wait_ge(zeroed, 4)
                step(layer, v.tensor_scalar(d, d, m, None, ALU.mult))
                settle(layer)
                if layer == 0:
                    rows = [(v1v[:, :, Q + 1 - dy, :, 0], v1v[:, :, Q + 1 - dy, :, 1], w1v[:, :, dy, :])
                            for dy in range(K1)]
                else:
                    rows = [(v2v[:, 0, :, WIN - K1 - dy, :], v2v[:, 1, :, WIN - K1 - dy, :], sq(wt)[:, :, dy, :])
                            for dy in range(K2)]
                    dve.wait_ge(zeroed, 11)
                for hi, lo, taps in rows:
                    step(layer, v.tensor_copy(hi, taps))
                settle(layer)
                for hi, lo, taps in rows:
                    step(layer, v.tensor_tensor(lo, taps, hi, ALU.subtract))
                assert done[layer] == PREP[layer]

            def take_scales(layer):
                dve.wait_ge(scales_summed, layer + 1)
                step(layer, v.tensor_scalar(SC[:, layer, :], PS[:, 7, layer * G:(layer + 1) * G],
                                            (1.0, 0.25)[layer] / (ZS * WS), None, ALU.mult))
                settle(layer)

            dve.wait_ge(taps_loaded[0], 16)
            prepare(0)
            take_scales(0)

            def finish(layer, u0, u):
                f, tmp, rb = fin[layer], TMP[:, layer], RB[:, layer, u0 % 2]
                mean, msq = ST[:, layer, :, 0], ST[:, layer, :, 1]
                steps = [0]

                def nxt(ins, wait=True):
                    steps[0] += 1
                    ins.then_inc(f, 1)
                    if wait:
                        dve.wait_ge(f, u * FIN + steps[0])

                dve.wait_ge(summed[layer], u + 1)
                if layer == 0:
                    nxt(v.tensor_copy(ST[:, 0, :, :], PST[:, 0:2 * NI].rearrange("p (i s) -> p i s", s=2)))
                else:
                    nxt(v.tensor_reduce(ST[:, 1, :, :], PST.rearrange("p (c i s) -> p i s c", c=CPU_, s=2), AXX,
                                        ALU.add))
                nxt(v.tensor_tensor(tmp[:, 0], mean, mean, ALU.mult))
                nxt(v.tensor_tensor(tmp[:, 1], msq, tmp[:, 0], ALU.subtract))
                nxt(v.tensor_scalar(tmp[:, 2], tmp[:, 1], 0.0, EPS, ALU.max, ALU.add))
                dve.wait_ge(root[layer], u + 1)
                nxt(v.reciprocal(tmp[:, 4], tmp[:, 3]))
                nxt(v.tensor_tensor(tmp[:, 0], tmp[:, 2], tmp[:, 4], ALU.mult))
                nxt(v.tensor_tensor(tmp[:, 1], tmp[:, 0], tmp[:, 4], ALU.mult))
                nxt(v.tensor_scalar(tmp[:, 5], tmp[:, 1], -0.5, 1.5, ALU.mult, ALU.add))
                nxt(v.scalar_tensor_tensor(rb[:, 0], tmp[:, 4], ZS, tmp[:, 5], ALU.mult, ALU.mult))
                nxt(v.scalar_tensor_tensor(rb[:, 1], mean, -1.0, rb[:, 0], ALU.mult, ALU.mult))
                assert steps[0] == FIN

            def add_conv2(n, at):
                if real(n):
                    c = n % CPU_
                    g = at(n - n % GCH) // GCH
                    dve.wait_ge(conv2_done, at(n) + 1)
                    for first, last, signal in ((CC - 1, CC, bank_free), (0, CC - 1, out_done)):
                        y = X[:, ring(n), c * CC + first:c * CC + last, :, :].rearrange("p c i w -> p (c i w)")
                        v.scalar_tensor_tensor(y, banks2(n)[:, first:last].rearrange("p b w -> p (b w)"),
                                               SC[:, 1, bass.ds(g, 1)], y, ALU.mult, ALU.add).then_inc(signal, 1)

            def slot(t, at):
                if t <= NCH:
                    add_conv2(t - 5, at)
                n = t - 3
                if real(n) and n % CPU_ == 0:
                    finish(1, n // CPU_, at(n) // CPU_)
                if real(n):
                    for img in range(NI):
                        m = NI * at(n) + img
                        dve.wait_ge(normed[1], m + 1)
                        dve.wait_ge(hi_done[1], m + 1)
                        v.tensor_tensor(part(H2, n, 1, img, O2, P2),
                                        Z[:, img, :].rearrange("p (c w) -> p c w", c=CC),
                                        part(H2, n, 0, img, O2, P2), ALU.subtract).then_inc(lo_done[1], 1)
                n = t + 1
                if real(n) and n % CPU_ == 0:
                    finish(0, n // CPU_, at(n) // CPU_)
                if real(n):
                    for img in range(NI):
                        m = NI * at(n) + img
                        dve.wait_ge(normed[0], m + 1)
                        dve.wait_ge(hi_done[0], m + 1)
                        v.tensor_tensor(part(H1, n, 1, img, O1, P1),
                                        Z[:, img, :].rearrange("p (c w) -> p c w", c=CC),
                                        part(H1, n, 0, img, O1, P1), ALU.subtract).then_inc(lo_done[0], 1)
                if t == 1:
                    take_scales(1)
                n = t
                if real(n):
                    c = n % CPU_
                    g = at(n - n % GCH) // GCH
                    dve.wait_ge(conv1_done, at(n) + 1)
                    for img in range(NI):
                        v.scalar_tensor_tensor(xs(n, img), PA[:, :, img * W:(img + 1) * W],
                                               SC[:, 0, bass.ds(g, 1)], xs(n, img), ALU.mult, ALU.add,
                                               accum_out=SS[:, c, img, 0:1]).then_inc(y_done, 1)
                n = t + 4
                if real(n):
                    c = n % CPU_
                    dve.wait_ge(x_loaded[n % BODY], (at(n - n % BODY) // BODY + 1) * (16 * NI))
                    for img in range(NI):
                        v.bn_stats(BN[:, c, img, :], xs(n, img)).then_inc(bn_done, 1)
                    if c == CPU_ - 1:
                        wait_apart(dve, bn_done, NI * at(n) + NI)
                        u = at(n - c) // CPU_
                        for img in range(NI):
                            v.bn_aggr(MQ1[:, img, :], BN[:, :, img, :]).then_inc(mq_ready, 1)
                        dve.wait_ge(mq_ready, u * (NI + 2) + NI)
                        v.tensor_tensor(TMP[:, 0, 0], MQ1[:, :, 0], MQ1[:, :, 0], ALU.mult).then_inc(mq_ready, 1)
                        dve.wait_ge(mq_ready, u * (NI + 2) + NI + 1)
                        v.tensor_tensor(MQ1[:, :, 1], MQ1[:, :, 1], TMP[:, 0, 0], ALU.add).then_inc(mq_ready, 1)
                if t > NCH:
                    add_conv2(t - 5, at)
                if t == -1:
                    dve.wait_ge(taps_loaded[1], 16)
                    add_rotations()
                if t == 0:
                    prepare(1)

            walk(dve, slot)

        @block.scalar
        def _(act):
            def normalise(layer, n, at):
                m = NI * at(n)
                for img in range(NI):
                    if layer == 1 and real(n + 3):
                        act.wait_ge(lo_done[0], m + 3 * NI + img + 1)
                    elif layer == 1:
                        act.wait_ge(lo_done[1], m - NI + img + 1)
                    elif real(n - 4):
                        act.wait_ge(lo_done[1], m - 4 * NI + img + 1)
                    elif n > 0:
                        act.wait_ge(lo_done[0], m - NI + img + 1)
                    rb = RB[:, layer, (n // CPU_) % 2]
                    nc.scalar.activation(Z[:, img, :].rearrange("p (c w) -> p c w", c=CC), xs(n, img),
                                         ACT.Identity, bias=rb[:, 1, img:img + 1],
                                         scale=rb[:, 0, img:img + 1]).then_inc(normed[layer], 1)

            def take_root(layer, u):
                act.wait_ge(fin[layer], u * FIN + 4)
                nc.scalar.activation(TMP[:, layer, 3], TMP[:, layer, 2], ACT.Sqrt).then_inc(root[layer], 1)

            def slot(t, at):
                n = t - 1
                if real(n):
                    for img in range(NI):
                        act.wait_ge(y_done, NI * at(n) + img + 1)
                        if n > 0 or img >= 2:
                            act.wait_ge(squared, NI * at(n) + img - 1)
                        nc.scalar.activation(DUMP[:, img % 2].rearrange("p (c w) -> p c w", c=CC), xs(n, img),
                                             ACT.Square, accum_out=SS[:, n % CPU_, img, 1:2]).then_inc(squared, 1)
                n = t - 3
                if real(n):
                    if n % CPU_ == 0:
                        take_root(1, at(n) // CPU_)
                        act.wait_ge(fin[1], (at(n) // CPU_) * FIN + FIN)
                    normalise(1, n, at)
                n = t + 1
                if real(n):
                    if n % CPU_ == 0:
                        take_root(0, at(n) // CPU_)
                        act.wait_ge(fin[0], (at(n) // CPU_) * FIN + FIN)
                    normalise(0, n, at)

            walk(act, slot)

        @block.gpsimd
        def _(pool):
            g = nc.gpsimd
            g.memset(v1_sb.bitcast(F32), 0.0).then_inc(zeroed, 1)
            g.memset(diag, 0.0).then_inc(zeroed, 1)
            pool.wait_ge(zeroed, 2)
            for k in range(2):
                d = diag[:, k * G:(k + 1) * G]
                g.affine_select(out=d, in_=d, compare_op=ALU.not_equal, fill=1.0, base=0, pattern=[[-1, G]],
                                channel_multiplier=1).then_inc(zeroed, 1)
            g.memset(onesg, 1.0).then_inc(zeroed, 1)
            g.memset(ONES1[:], 1.0 / P).then_inc(zeroed, 1)
            g.memset(ONES2[:], 1.0 / (GC * P * W)).then_inc(zeroed, 1)
            for whole in (BAND1[:], H1[:], H2[:], v2_sb):
                g.memset(flat32(whole), 0.0).then_inc(zeroed, 1)
            pool.wait_ge(zeroed, 11)

            def high_parts(layer, n, at):
                H, off, pitch = ((H1, O1, P1), (H2, O2, P2))[layer]
                u = at(n - n % CPU_) // CPU_
                wait_apart(pool, fin[layer], u * FIN + FIN)
                if n >= 2:
                    if layer == 0:
                        wait_apart(pool, conv1_done, at(n) - 1)
                    else:
                        wait_apart(pool, gathered[n % 2], ((at(n) - n % 2) // 2) * (16 * 3 * NB))
                rb = RB[:, layer, (n // CPU_) % 2]
                for img in range(NI):
                    g.tensor_scalar(part(H, n, 0, img, off, pitch), xs(n, img), rb[:, 0, img:img + 1],
                                    rb[:, 1, img:img + 1], ALU.mult, ALU.add).then_inc(hi_done[layer], 1)

            def slot(t, at):
                if real(t - 3):
                    high_parts(1, t - 3, at)
                if real(t + 1):
                    high_parts(0, t + 1, at)
                if t == 1:
                    pool.wait_ge(vectors_stored[1], 16)
                    g.memset(flat32(BT[:]), 0.0).then_inc(blocks_zeroed, 1)

            walk(pool, slot)

        @block.tensor
        def _(pe):
            mm = nc.tensor.matmul

            def spread_scales(layer):
                pe.wait_ge(prep[layer], PREP[layer])
                cols = slice(layer * G, (layer + 1) * G)
                mm(PS[:, 7, cols], onesg, diag[:, cols], start=True, stop=True).then_inc(scales_summed, 1)
                pe.wait_ge(prep[layer], PREP[layer] + 1)

            pe.wait_ge(zeroed, 7)
            spread_scales(0)

            def slot(t, at):
                n = t
                for ch in range(CC):
                    if ch == 1:
                        u = t - 3
                        if real(u) and u % CPU_ == 0:
                            pe.wait_ge(squared, NI * at(u) + NI * CPU_)
                            if real(t - 5):
                                pe.wait_ge(bank_free, at(t - 5) + 1)
                            mm(PST, ONES2[:], SS[:].rearrange("p c i s -> p (c i s)"), start=True,
                               stop=True).then_inc(summed[1], 1)
                        u = t + 1
                        if real(u) and u % CPU_ == 0:
                            pe.wait_ge(mq_ready, (at(u) // CPU_ + 1) * (NI + 2))
                            if real(t - 5):
                                pe.wait_ge(bank_free, at(t - 5) + 1)
                            mm(PST[:, 0:2 * NI], ONES1[:], MQ1[:].rearrange("p i s -> p (i s)"), start=True,
                               stop=True).then_inc(summed[0], 1)
                    if not real(n):
                        continue
                    c = n % CPU_
                    if ch == 0:
                        pe.wait_ge(band1_loaded[c], (at(n - n % GCH) // GCH) * 64 + 64)
                        pe.wait_ge(lo_done[0], NI * at(n) + NI)
                        if n >= 1:
                            pe.wait_ge(y_done, NI * at(n))
                    band = BAND1[:, c * CC + ch, :].rearrange("p (m j s) -> p j s m", m=P, j=K1)
                    k = 0
                    for j in range(K1):
                        for which, ws in ((0, 0), (1, 0), (0, 1)):
                            data = H1[:, n % 2, which, ch, :].rearrange("p (i q) -> p i q", i=NI)
                            last = mm(PA[:, ch, :], band[:, j, ws, :], data[:, :, O1 - 1 + j:O1 - 1 + j + W],
                                      start=k == 0, stop=k == 3 * K1 - 1)
                            k += 1
                    if ch == CC - 1:
                        last.then_inc(conv1_done, 1)
                if t == 1:
                    spread_scales(1)
                n = t - 4
                if real(n):
                    c = n % CPU_
                    pe.wait_ge(band2_loaded[c], (at(n - n % GCH) // GCH) * 16 + 16)
                    pe.wait_ge(gathered[n % 2], ((at(n) - n % 2) // 2 + 1) * (16 * 3 * NB))
                    if n == NCH - CONV2:
                        pe.wait_ge(y_done, NI * NCH)
                    elif n > NCH - CONV2:
                        pe.wait_ge(out_done, n - 1)
                    elif n >= 1:
                        pe.wait_ge(out_done, at(n))
                    for ch in range(CC):
                        if ch == CC - 1:
                            if real(t - 3) and (t - 3) % CPU_ == 0:
                                pe.wait_ge(fin[1], (at(t - 3) // CPU_) * FIN + 1)
                            if real(t + 1) and (t + 1) % CPU_ == 0:
                                pe.wait_ge(fin[0], (at(t + 1) // CPU_) * FIN + 1)
                        band = BAND2[0:3 * WIN, c * CC + ch, :].rearrange("p (m j) -> p j m", m=BL)
                        for j in range(K2):
                            for b in range(NB):
                                rows = BT[0:3 * WIN, n % 2, b, ch, O2 - K2 // 2 + j:]
                                rows = bass.AP(rows.tensor, rows.offset, [rows.ap[0], [P2, NI], [1, W]])
                                last = mm(banks2(n)[b * BL:(b + 1) * BL, ch, :], band[:, j, :],
                                          rows, start=j == 0, stop=j == K2 - 1, tile_position=(0, b * BL))
                    last.then_inc(conv2_done, 1)

            walk(pe, slot)


def kernel(**inputs):
    import numpy as _np
    import concourse.bacc as _bacc
    from concourse import mybir as _mybir
    from concourse.bass_utils import run_bass_kernel_spmd as _run

    nc = _bacc.Bacc("TRN2", target_bir_lowering=False, num_devices=1)
    arrays, args = {}, []
    for name in ("x", "L0_conv_k", "L1_conv_weight"):
        a = _np.ascontiguousarray(inputs[name])
        arrays[f"in_{name}"] = a
        args.append(nc.dram_tensor(f"in_{name}", a.shape, _mybir.dt.from_np(a.dtype), kind="ExternalInput").ap())
    shape = tuple(inputs["x"].shape)
    args.append(nc.dram_tensor("out_y", shape, _mybir.dt.float32, kind="ExternalOutput").ap())
    conv_program(nc, *args)
    r = _run(nc, [arrays], core_ids=[0])
    return r.results[0]["out_y"]
```
